# Optimizing a Trainium2 kernel written in Bass

```python
import numpy as np
import jax
import jax.numpy as jnp

def _softmax(x, axis=-1):
    return jax.nn.softmax(x, axis=axis)
def _gelu(x):
    return jax.nn.gelu(x, approximate=True)
def _silu(x):
    return jax.nn.silu(x)
def _sigmoid(x):
    return jax.nn.sigmoid(x)
def _layernorm(x, axis=-1, eps=1e-5):
    m = jnp.mean(x, axis=axis, keepdims=True)
    v = jnp.var(x, axis=axis, keepdims=True)
    return (x - m) / jnp.sqrt(v + eps)
def _scatter_add(tgt, idx, src, axis=0):
    return tgt.at[idx].add(src)
def _segment_sum(src, seg, n):
    return jax.ops.segment_sum(src, seg, n)

kernel_name = 'mk_conv_attn_hybrid_d2_conv_nchw128_6d66e5'

def setup_inputs(seed: int = 0):
    np.random.seed(seed)
    _w = jnp.asarray
    def _rec_inputs():
        import jax
        import jax.numpy as jnp
        _gk = jax.random.key(seed)
        x = -0.0005153 + 1.001 * jax.random.normal(jax.random.fold_in(_gk, 1), (8, 128, 56, 56), jnp.float32)
        return x
    x = _rec_inputs()
    def _L0_conv_setup():
        import jax, jax.numpy as jnp
        import numpy as np
        K = 3
        STRIDE = 1
        PAD = 1

        def _conv2d(x, w, stride, pad):
            return jax.lax.conv_general_dilated(x, w, window_strides=(stride, stride), padding=((pad, pad), (pad, pad)), dimension_numbers=('NCHW', 'OIHW', 'NCHW'))
        key = jax.random.key(seed)
        k1, k2, k3, k4 = jax.random.split(key, 4)
        B, C, H, W = (8, 128, 56, 56)
        OUT = 128
        x = jax.random.normal(k1, (B, C, H, W), jnp.float32)
        offset_w = jax.random.normal(k2, (2 * K * K, C, K, K), jnp.float32) * 0.01
        offset_b = jax.random.normal(k3, (2 * K * K,), jnp.float32) * 0.01
        conv_w = jax.random.normal(k4, (OUT, C, K, K), jnp.float32) * 0.02
        return {'x': x, 'offset_w': offset_w, 'offset_b': offset_b, 'conv_w': conv_w}
    _L0_conv_all = _L0_conv_setup()
    _L0_conv_in = {k: v for k, v in _L0_conv_all.items() if k in ('offset_w', 'offset_b', 'conv_w', )}
    del _L0_conv_all

    def _L1_attn_setup():
        import jax, jax.numpy as jnp
        import numpy as np
        B, T, C = (16, 2048, 128)
        HEAD_SIZE = 128
        key = jax.random.key(seed)
        k1, k2, k3, k4 = jax.random.split(key, 4)
        x = jax.random.normal(k1, (B, T, C), dtype=jnp.float32)
        scale = (1.0 / np.sqrt(C)).astype(np.float32)
        Wq = jax.random.normal(k2, (HEAD_SIZE, C), dtype=jnp.float32) * scale
        Wk = jax.random.normal(k3, (HEAD_SIZE, C), dtype=jnp.float32) * scale
        Wv = jax.random.normal(k4, (HEAD_SIZE, C), dtype=jnp.float32) * scale
        return {'x': x, 'Wq': Wq, 'Wk': Wk, 'Wv': Wv}
    _L1_attn_all = _L1_attn_setup()
    _L1_attn_in = {k: v for k, v in _L1_attn_all.items() if k in ('Wq', 'Wk', 'Wv', )}
    del _L1_attn_all

    def _L1_ffn_setup():
        import jax, jax.numpy as jnp
        import numpy as np
        B, S, D, E, H, O, K = (512, 2048, 128, 64, 512, 128, 8)
        key = jax.random.key(seed)
        k0, k1, k2, k3 = jax.random.split(key, 4)
        x = jax.random.normal(k0, (B, S, D), dtype=jnp.float32)
        gate_w = jax.random.normal(k1, (E, D), dtype=jnp.float32) * (1.0 / np.sqrt(D))
        gate_b = jnp.zeros((E,), dtype=jnp.float32)
        weight1 = jax.random.uniform(k2, (E, D + 1, H), dtype=jnp.float32, minval=-1.0, maxval=1.0) * (1.0 / np.sqrt(D + 1))
        weight2 = jax.random.uniform(k3, (E, H + 1, O), dtype=jnp.float32, minval=-1.0, maxval=1.0) * (1.0 / np.sqrt(H + 1))
        return {'x': x, 'gate_w': gate_w, 'gate_b': gate_b, 'weight1': weight1, 'weight2': weight2}
    _L1_ffn_all = _L1_ffn_setup()
    _L1_ffn_in = {k: v for k, v in _L1_ffn_all.items() if k in ('gate_w', 'gate_b', 'weight1', 'weight2', )}
    del _L1_ffn_all

    return {
        "x": x,
        "L0_conv_offset_w": _L0_conv_in["offset_w"],
        "L0_conv_offset_b": _L0_conv_in["offset_b"],
        "L0_conv_conv_w": _L0_conv_in["conv_w"],
        "L1_attn_Wq": _L1_attn_in["Wq"],
        "L1_attn_Wk": _L1_attn_in["Wk"],
        "L1_attn_Wv": _L1_attn_in["Wv"],
        "L1_ffn_gate_w": _L1_ffn_in["gate_w"],
        "L1_ffn_gate_b": _L1_ffn_in["gate_b"],
        "L1_ffn_weight1": _L1_ffn_in["weight1"],
        "L1_ffn_weight2": _L1_ffn_in["weight2"],
    }

def reference(x, L0_conv_offset_w, L0_conv_offset_b, L0_conv_conv_w, L1_attn_Wq, L1_attn_Wk, L1_attn_Wv, L1_ffn_gate_w, L1_ffn_gate_b, L1_ffn_weight1, L1_ffn_weight2):
    import jax
    import jax.numpy as jnp
    def _L0_conv_ref(x, offset_w, offset_b, conv_w):
        import jax, jax.numpy as jnp
        import numpy as np
        K = 3
        STRIDE = 1
        PAD = 1

        def _conv2d(x, w, stride, pad):
            return jax.lax.conv_general_dilated(x, w, window_strides=(stride, stride), padding=((pad, pad), (pad, pad)), dimension_numbers=('NCHW', 'OIHW', 'NCHW'))
        n = K * K
        offset = _conv2d(x, offset_w, STRIDE, K // 2) + offset_b[None, :, None, None]
        b, _, h, w = offset.shape
        xp = jnp.pad(x, ((0, 0), (0, 0), (PAD, PAD), (PAD, PAD)))
        c, Hp, Wp = (xp.shape[1], xp.shape[2], xp.shape[3])
        r = jnp.arange(-(K // 2), K // 2 + 1, dtype=jnp.float32)
        py_n, px_n = jnp.meshgrid(r, r, indexing='ij')
        pn = jnp.concatenate([py_n.ravel(), px_n.ravel()])
        gy = jnp.arange(K // 2, h * STRIDE + 1, STRIDE, dtype=jnp.float32)
        gx = jnp.arange(K // 2, w * STRIDE + 1, STRIDE, dtype=jnp.float32)
        p0y, p0x = jnp.meshgrid(gy, gx, indexing='ij')
        p0 = jnp.concatenate([jnp.broadcast_to(p0y, (n, h, w)), jnp.broadcast_to(p0x, (n, h, w))], axis=0)[None]
        p = p0 + pn[None, :, None, None] + offset
        p = jnp.transpose(p, (0, 2, 3, 1))
        q = jax.lax.stop_gradient(jnp.floor(p))
        qlt_y = jnp.clip(q[..., :n], 0, Hp - 1)
        qlt_x = jnp.clip(q[..., n:], 0, Wp - 1)
        qrb_y = jnp.clip(q[..., :n] + 1, 0, Hp - 1)
        qrb_x = jnp.clip(q[..., n:] + 1, 0, Wp - 1)
        py = jnp.clip(p[..., :n], 0, Hp - 1)
        px = jnp.clip(p[..., n:], 0, Wp - 1)
        g_lt = (1 - (py - qlt_y)) * jnp.trunc(1 - (px - qlt_x))
        g_rb = (1 - (qrb_y - py)) * jnp.trunc(1 - (qrb_x - px))
        g_lb = (1 - (py - qlt_y)) * (1 - (qrb_x - px))
        g_rt = (1 - (qrb_y - py)) * (1 - (px - qlt_x))
        x_flat = xp.reshape(b, c, Hp * Wp)

        def gather(qy, qx):
            idx = (qy * Wp + qx).astype(jnp.int32).reshape(b, 1, -1)
            out = jnp.take_along_axis(x_flat, jnp.broadcast_to(idx, (b, c, idx.shape[-1])), axis=-1)
            return out.reshape(b, c, h, w, n)
        x_off = g_lt[:, None] * gather(qlt_y, qlt_x) + g_rb[:, None] * gather(qrb_y, qrb_x) + g_lb[:, None] * gather(qlt_y, qrb_x) + g_rt[:, None] * gather(qrb_y, qlt_x)
        x_off = x_off.reshape(b, c, h, w, K, K).transpose(0, 1, 2, 4, 3, 5).reshape(b, c, h * K, w * K)
        return _conv2d(x_off, conv_w, K, 0)

    def _L1_attn_ref(x, Wq, Wk, Wv):
        import jax, jax.numpy as jnp
        import numpy as np
        B, T, C = (16, 2048, 128)
        HEAD_SIZE = 128
        Bd, Td, Cd = x.shape
        q = jnp.einsum('btc,hc->bth', x, Wq)
        k = jnp.einsum('btc,hc->bth', x, Wk)
        v = jnp.einsum('btc,hc->bth', x, Wv)
        scores = jnp.einsum('bth,bsh->bts', q, k) * Cd ** (-0.5)
        causal = jnp.tril(jnp.ones((Td, Td), dtype=bool))
        scores = jnp.where(causal, scores, -jnp.inf)
        attn = jax.nn.softmax(scores, axis=-1)
        out = jnp.einsum('bts,bsh->bth', attn, v)
        return out

    def _L1_ffn_ref(x, gate_w, gate_b, weight1, weight2):
        import jax, jax.numpy as jnp
        import numpy as np
        B, S, D, E, H, O, K = (512, 2048, 128, 64, 512, 128, 8)
        Bn, Sn, Dn = x.shape
        logits = jnp.einsum('bsd,ed->bse', x, gate_w) + gate_b
        probs = jax.nn.softmax(logits, axis=1)
        vals, idx = jax.lax.top_k(probs.transpose(0, 2, 1), K)
        topv = vals.transpose(0, 2, 1)
        topi = idx.transpose(0, 2, 1)
        flat_idx = topi.reshape(Bn, K * E)
        gathered = jnp.take_along_axis(x, flat_idx[:, :, None], axis=1)
        gathered = gathered.reshape(Bn, K, E, Dn)
        pooled = jnp.einsum('bked,bke->bed', gathered, topv)
        ones = jnp.ones((E, Bn, 1), dtype=x.dtype)
        h = jnp.concatenate([pooled.transpose(1, 0, 2), ones], axis=-1)
        h = jax.nn.gelu(jnp.einsum('ebd,edh->ebh', h, weight1), approximate=False)
        h = jnp.concatenate([h, ones], axis=-1)
        out = jnp.einsum('ebh,eho->ebo', h, weight2)
        out = out.transpose(1, 0, 2)
        weighted = jnp.einsum('beo,bke->bkeo', out, topv).reshape(Bn, K * E, O)
        outputs = jnp.zeros((Bn, Sn, O), dtype=x.dtype)
        outputs = outputs.at[jnp.arange(Bn)[:, None], flat_idx].add(weighted)
        return outputs

    def _gn(v, G=32, eps=1e-5):
        B_, C_, H_, W_ = v.shape
        g = v.reshape(B_, G, C_ // G, H_, W_)
        m = jnp.mean(g, axis=(2, 3, 4), keepdims=True)
        s = jnp.var(g, axis=(2, 3, 4), keepdims=True)
        return ((g - m) / jnp.sqrt(s + eps)).reshape(v.shape)

    def _ln_c(v, eps=1e-6):
        m = jnp.mean(v, axis=1, keepdims=True)
        s = jnp.var(v, axis=1, keepdims=True)
        return (v - m) / jnp.sqrt(s + eps)

    def _ln_t(v, eps=1e-5):
        m = jnp.mean(v, axis=-1, keepdims=True)
        s = jnp.var(v, axis=-1, keepdims=True)
        return (v - m) / jnp.sqrt(s + eps)

    def _to_tokens(v):
        B_, C_, H_, W_ = v.shape
        return v.reshape(B_, C_, H_ * W_).transpose(0, 2, 1)
    def _from_tokens(t, like):
        B_, C_, H_, W_ = like.shape
        return t.transpose(0, 2, 1).reshape(B_, C_, H_, W_)

    x = x + _L0_conv_ref(_gn(x), L0_conv_offset_w, L0_conv_offset_b, L0_conv_conv_w)
    t = _to_tokens(x)
    t = t + _L1_attn_ref(_ln_t(t), L1_attn_Wq, L1_attn_Wk, L1_attn_Wv)
    t = t + _L1_ffn_ref(_ln_t(t), L1_ffn_gate_w, L1_ffn_gate_b, L1_ffn_weight1, L1_ffn_weight2)
    x = _from_tokens(t, x)
    return x


_drawn_inputs = setup_inputs


def setup_inputs(seed=0):
    import zlib

    import numpy as np

    out = dict(_drawn_inputs(seed))
    spreads = {'L1_ffn_gate_b': (0.0, 0.1)}
    factors = {'L1_ffn_gate_w': 8.0, 'L1_ffn_weight1': 8.0, 'L1_ffn_weight2': 8.0}
    for name, (base, spread) in spreads.items():
        noise = np.random.default_rng([zlib.crc32(name.encode()), seed]).standard_normal(out[name].shape)
        drawn = base * np.exp(spread * noise) if base else spread * noise
        out[name] = jnp.asarray(drawn.astype(out[name].dtype))
    for name, factor in factors.items():
        out[name] = (out[name] * factor).astype(out[name].dtype)
    return out
```

```python
from contextlib import ExitStack

import numpy as np

import concourse.bass as bass
from concourse import mybir

F32 = mybir.dt.float32
I32 = mybir.dt.int32
U32 = mybir.dt.uint32
ALU = mybir.AluOpType
ACT = mybir.ActivationFunctionType
AXX = mybir.AxisListType.X

P = 128
B, C, H, W = 8, 128, 56, 56
N = H * W
TILES = -(-N // P)
NP = TILES * P
LAST = N - (TILES - 1) * P
HP, WP = H + 2, W + 2
TAPS = 9
E = 64
TOP = 8
HID = 512
SCALE = float(C) ** -0.5
GROUPS = 32
CHUNK = 512
LX = W + NP + W
ROWS = 2 * HP * WP
RING = 5
PIECES = 3
assert TILES % RING == 0 and TAPS == 3 * PIECES
ZEROED = 6 + RING
STATS = 7
NEG = -3.0e38
EPS = 1e-5
RSQRT_GUESS = float(0x5f3759df - (2 << 23))
OFFSETS_PER_STEP = 2
OFFSET_STEP0 = 4
STATS_STEP, NORM_STEP, INDEX_STEP = 1, 2, 18


def chunks_of(i):
    total = (i + 1) * P
    return [(k, min(CHUNK, total - k)) for k in range(0, total, CHUNK)]


def chunks_before(i):
    return sum(len(chunks_of(t)) for t in range(i))


ALL_CHUNKS = chunks_before(TILES)


class Signal:

    def __init__(self, sem, per_image, unit=1, before=0):
        self.sem, self.per, self.unit, self.primed = sem, per_image, unit, before * unit + 1

    def at(self, image, n):
        return image * (self.per * self.unit) + (n * self.unit + self.primed)


class Link:

    def __init__(self, eng, count):
        self.eng, self.count, self.n, self.image = eng, count, 0, 0

    def start(self, image):
        self.image, self.n = image, 0

    def __call__(self, ins):
        ins.then_inc(self.count.sem, 1)
        self.n += 1
        self.eng.wait_ge(self.count.sem, self.count.at(self.image, self.n))


def hold(eng, held):
    eng.sem_inc(held, 1)


def hybrid_kernel(nc, x_cm, x_tok, off_w, off_b, conv_w, wq, wk, wv, gate_w, gate_b, w1, w2,
                  c_base, c_ident, c_mask, c_group, out):
    pair_table = [nc.dram_tensor(f"pair_table{r}", (ROWS, 2 * C), F32, kind="Internal").ap() for r in range(2)]
    t2_dram = nc.dram_tensor("t2_dram", (B, P, TILES, C), F32, kind="Internal").ap()
    pm_dram = nc.dram_tensor("pm_dram", (B, E, NP), F32, kind="Internal").ap()
    pooled_dram = nc.dram_tensor("pooled_dram", (B, E, C), F32, kind="Internal").ap()
    rz_dram = nc.dram_tensor("rz_dram", (B, E, 1), F32, kind="Internal").ap()
    with (
        nc.sbuf_tensor("b1_t", [P, E, 4], F32) as b1_t,
        nc.sbuf_tensor("b2", [E, C], F32) as b2,
        nc.sbuf_tensor("ident", [P, P], F32) as ident,
    ):
        first_part(nc, x_cm, x_tok, off_w, off_b, conv_w, wq, wk, wv, gate_w, gate_b, w1, w2, b1_t, b2, ident,
                   c_base, c_ident, c_mask, c_group, pair_table, t2_dram, pm_dram, pooled_dram, rz_dram)
        second_part(nc, w1, w2, b1_t, b2, ident, t2_dram, pm_dram, pooled_dram, rz_dram, out)


def first_part(nc, x_cm, x_tok, off_w, off_b, conv_w, wq, wk, wv, gate_w, gate_b, w1, w2, b1_t, b2, ident,
               c_base, c_ident, c_mask, c_group, pair_table, t2_dram, pm_dram, pooled_dram, rz_dram):
    with ExitStack() as ctx:
        def sb(name, shape, dt=F32):
            return ctx.enter_context(nc.sbuf_tensor(name, shape, dt))

        def psum(name, shape):
            return ctx.enter_context(nc.psum_tensor(name, shape, F32))

        def sem(name):
            return ctx.enter_context(nc.semaphore(name))

        def signal(name, per_image, unit=1, before=0):
            return Signal(sem(name), per_image, unit, before)

        mask = sb("mask", [P, CHUNK + P])
        group = sb("group", [P, P])
        base = sb("base", [P, TILES, 18])
        off_bias = sb("off_bias", [P, 18])
        gate_bias = sb("gate_bias", [E, 1])
        offw_t = sb("offw_t", [P, TAPS, 18])
        convw_t = sb("convw_t", [P, TAPS, P])
        wv_t = sb("wv_t", [P, P])
        wqk = sb("wqk", [P, P])
        gate_t = sb("gate_t", [P, E])
        xs = [sb(f"xs{d}", [P, LX]) for d in range(3)]
        bn = sb("bn", [P, STATS, 6])
        mv = sb("mv", [P, 2])
        gstat = sb("gstat", [P, 2])
        gvar = sb("gvar", [P, 13])
        rs_next = sb("rs_next", [P, 1])
        nb_next = sb("nb_next", [P, 2 * TAPS - 1])
        scratch = xs[1][:, W:W + 11 * TILES * TAPS]
        pos, qf, qi, tmp, fx1, eq, om = (
            scratch[:, a * TILES * TAPS:z * TILES * TAPS].rearrange("p (t k) -> p t k", t=TILES)
            for a, z in ((0, 2), (2, 4), (4, 6), (6, 8), (8, 9), (9, 10), (10, 11)))
        qi = qi.bitcast(I32)
        wa_next = sb("wa_next", [P, TILES, TAPS])
        wb_next = sb("wb_next", [P, TILES, TAPS])
        u_next = sb("u_next", [P, TILES, TAPS])
        idx_next = sb("idx_next", [P, TILES * TAPS], U32)
        rs = sb("rs", [P, 1])
        shift = sb("shift", [TAPS, P])
        wa = sb("wa", [P, TILES, TAPS])
        wb = sb("wb", [P, TILES, TAPS])
        u = sb("u", [P, TILES, TAPS])
        idx = sb("idx", [P, TILES * TAPS], U32)
        g = [sb(f"g{r}", [P, TAPS, 2 * C]) for r in range(RING)]
        xt = [sb(f"xt{r}", [P, C]) for r in range(RING)]
        smp = [sb(f"smp{r}", [P, TAPS, C]) for r in range(2)]
        smp_t = [sb(f"smp_t{r}", [P, 3 * P]) for r in range(PIECES)]
        u_t = [sb(f"u_t{r}", [TAPS, P]) for r in range(2)]
        t1 = [sb(f"t1_{r}", [P, C]) for r in range(3)]
        ln = [sb(f"ln{r}", [P, 13]) for r in range(2)]
        newton = sb("newton", [P, 3])
        xn = [sb(f"xn{r}", [P, C]) for r in range(2)]
        keys = sb("keys", [P, NP])
        vals = sb("vals", [P, TILES, P])
        qt = [sb(f"qt{r}", [P, P]) for r in range(2)]
        prob = [sb(f"prob{r}", [P, NP]) for r in range(2)]
        cmax = [sb(f"cmax{r}", [P, 8]) for r in range(2)]
        nmax = [sb(f"nmax{r}", [P, 2]) for r in range(2)]
        total = [sb(f"total{r}", [P, 1]) for r in range(2)]
        prob_t = [sb(f"prob_t{r}", [P, CHUNK]) for r in range(2)]
        t2 = [sb(f"t2_{r}", [P, C]) for r in range(3)]
        xf = sb("xf", [P, TILES, C])
        xf_t = sb("xf_t", [P, P])
        logit = sb("logit", [E, NP])
        rest = prob[0][0:E, 0:N]
        lmax = sb("lmax", [E, 2])
        zsum = sb("zsum", [E, 1])
        rz = sb("rz", [E, 1])
        top = sb("top", [E, TOP])
        raw_off, raw_conv = prob[1][0:18, 0:TAPS * C], prob[1][:, TAPS * C:2 * TAPS * C]
        pm_tok = prob[1][:, 0:TILES * E].rearrange("p (t e) -> p t e", e=E)
        pooled = sb("pooled", [E, C])

        bank_off = psum("bank_off", [P, 512])
        bank_conv = psum("bank_conv", [P, 512])
        bank_proj = psum("bank_proj", [P, 512])
        bank_t = [psum(f"bank_t{r}", [P, 512]) for r in range(2)]
        bank_s = [psum(f"bank_s{r}", [P, 512]) for r in range(2)]
        bank_o = psum("bank_o", [P, 512])
        off_ps = bank_off[:, 0:TILES * 18].rearrange("p (t k) -> p t k", k=18)
        conv_ps, small_ps = bank_conv[:, 0:P], bank_conv[:, P:2 * P]
        xnt_ps, val_ps = bank_proj[:, 0:P], bank_proj[:, P:2 * P]
        qt_ps, xft_ps, logit_ps = bank_proj[:, 2 * P:3 * P], bank_proj[:, 3 * P:], bank_proj[0:E, 0:P]

        held_sp1 = sem("held_sp1")
        held_pool, held_pe, held_dve = sem("held_pool"), sem("held_pe"), sem("held_dve")
        weights_in, zeroed, border_in = sem("weights_in"), sem("zeroed"), sem("border_in")
        setup_mm, setup_ev = sem("setup_mm"), sem("setup_ev")
        x_in = signal("x_in", 1, 16)
        table_in = signal("table_in", 4, 16)
        gathered = [signal(f"gathered{r}", TILES // RING * TAPS, 16) for r in range(RING)]
        for sig in gathered:
            sig.primed = 0
        xt_in = [signal(f"xt_in{r}", TILES // RING, 16) for r in range(RING)]
        t2_out = [signal(f"t2_out{r}", len(range(r, TILES, 3)), 16) for r in range(3)]
        route_out = signal("route_out", 3, 16)
        stats_done = signal("stats_done", 1)
        gstat_done = signal("gstat_done", 1)
        affine_done = signal("affine_done", 1)
        shifted = signal("shifted", 1)
        offsets_done = signal("offsets_done", 1)
        indexed = signal("indexed", 1)
        shift_mm = signal("shift_mm", 1)
        shift_ev = signal("shift_ev", 1)
        idx_copied = signal("idx_copied", 1)
        rs_copied = signal("rs_copied", 1)
        u_copied = signal("u_copied", 1)
        scaled = signal("scaled", TILES)
        sampled = signal("sampled", TILES * PIECES, before=PIECES * RING)
        smp_tp = signal("smp_tp", TILES * PIECES)
        smp_ev = signal("smp_ev", TILES * PIECES)
        conv_done = signal("conv_done", TILES)
        normed = signal("normed", TILES)
        xnt_tp = signal("xnt_tp", TILES)
        xnt_ev = signal("xnt_ev", TILES)
        proj_done = signal("proj_done", TILES)
        proj_ev = signal("proj_ev", TILES)
        scored = signal("scored", ALL_CHUNKS)
        score_ev = signal("score_ev", ALL_CHUNKS)
        max_done = signal("max_done", TILES)
        exp_done = signal("exp_done", TILES)
        prob_tp = signal("prob_tp", ALL_CHUNKS)
        prob_ev = signal("prob_ev", ALL_CHUNKS)
        attended = signal("attended", TILES)
        normed2 = signal("normed2", TILES)
        xft_tp = signal("xft_tp", TILES)
        xft_ev = signal("xft_ev", TILES)
        logit_mm = signal("logit_mm", TILES)
        logit_ev = signal("logit_ev", TILES)
        lmax_done = signal("lmax_done", 1)
        lexp_done = signal("lexp_done", 1)
        chosen = signal("chosen", 1)
        rz_done = signal("rz_done", 1)
        PMG = -(-TILES // 8)
        pm_tp = signal("pm_tp", PMG)
        pm_ev = signal("pm_ev", PMG)
        pooled_mm = signal("pooled_mm", 1)
        pooled_ev = signal("pooled_ev", 1)
        RSQRT_LINKS = 8
        ADVE_STATS, ADVE_AFFINE, ADVE_INDEX = 2, 4 + RSQRT_LINKS, 24
        link_prep = signal("link_prep", ADVE_STATS + ADVE_AFFINE + ADVE_INDEX)
        link_norm = signal("link_norm", (3 + RSQRT_LINKS) * TILES)
        link_max = signal("link_max", TILES)
        link_norm2 = signal("link_norm2", (4 + RSQRT_LINKS) * TILES)
        link_route = signal("link_route", 3)
        link_xs = signal("link_xs", 2)

        ring_order = []
        for s in range(TILES + 3):
            if s < TILES:
                ring_order += [(smp_ev, PIECES * s + p) for p in range(PIECES)]
            if 0 <= s - 2 < TILES:
                ring_order += [(prob_ev, chunks_before(s - 2) + j) for j in range(len(chunks_of(s - 2)))]
        ring_at = {(sig is smp_ev, n): q for q, (sig, n) in enumerate(ring_order)}

        def ring_use(is_smp, n):
            return bank_t[ring_at[is_smp, n] % 2]

        def wait_ring(pe, b, is_smp, n):
            q = ring_at[is_smp, n]
            if q >= 2:
                sig, m = ring_order[q - 2]
                pe.wait_ge(sig.sem, sig.at(b, m + 1))
            else:
                for sig, per in ((smp_ev, TILES * PIECES), (prob_ev, ALL_CHUNKS)):
                    pe.wait_ge(sig.sem, sig.at(b, 0))

        block = ctx.enter_context(nc.Block())

        @block.sync
        def _(sp):
            for dst, src in ((ident[:], c_ident), (mask[:], c_mask), (group[:], c_group),
                             (base[:], c_base.rearrange("p (t k) -> p t k", k=18)),
                             (off_bias[:], off_b.unsqueeze(0).broadcast_to([P, 18])),
                             (gate_bias[:], gate_b.rearrange("(e a) -> e a", a=1)),
                             (raw_off, off_w.rearrange("o c a k -> o (c a k)")),
                             (raw_conv, conv_w.rearrange("o c a k -> o (c a k)")),
                             (vals[:, 0, :], wq), (vals[:, 1, :], wk), (vals[:, 2, :], wv),
                             (vals[0:E, 3, :], gate_w),
                             (b1_t[:], w1[:, C, :].rearrange("e (p j) -> p e j", j=4)),
                             (b2[:], w2[:, HID, :])):
                sp.dma_start(dst, src).then_inc(weights_in, 16)
            for sig in (x_in, table_in, route_out, *xt_in, *t2_out):
                sp.sem_inc(sig.sem, sig.primed)
            sp.wait_ge(zeroed, ZEROED)
            table = [t.rearrange("(v y x) (h c) -> v y x h c", v=2, y=HP, h=2) for t in pair_table]
            zero = prob[0][0:HP, 0:C]
            for rows in table:
                for v in range(2):
                    for h in range(2):
                        y0, x0 = (1, v) if h == 0 else (0, 1)
                        for y in [r for r in range(HP) if not y0 <= r < y0 + H]:
                            sp.dma_start(rows[v, y, :, h, :], zero).then_inc(border_in, 16)
                        for x in [r for r in range(WP) if not x0 <= r < x0 + W]:
                            sp.dma_start(rows[v, y0:y0 + H, x, h, :], zero[0:H, :]).then_inc(border_in, 16)

            def load_image(k, at, parity):
                sp.wait_ge(indexed.sem, indexed.at(k, 0))
                sp.dma_start(xs[1][:, W:W + N], x_cm[bass.ds(at, 1)].rearrange("a c n -> (a c) n"))\
                  .then_inc(x_in.sem, 16)
                src = x_tok[bass.ds(at * N, N)].rearrange("(y x) c -> y x c", x=W)
                for v in range(2):
                    for h in range(2):
                        y0, x0 = (1, v) if h == 0 else (0, 1)
                        sp.dma_start(table[parity][v, y0:y0 + H, x0:x0 + W, h, :], src).then_inc(table_in.sem, 16)

            load_image(0, 0, 0)
            with sp.Fori(0, B // 2) as half:
              for parity in range(2):
                b = half * 2 + parity
                for s in range(TILES + 2):
                    if s < TILES:
                        if s >= RING:
                            sp.wait_ge(normed.sem, normed.at(b, s - RING + 1))
                        else:
                            sp.wait_ge(normed.sem, normed.at(b, 0))
                        rows = P if s < TILES - 1 else LAST
                        sp.dma_start(xt[s % RING][0:rows, :], x_tok[bass.ds(b * N + s * P, rows)])\
                          .then_inc(xt_in[s % RING].sem, 16)
                    if s == 1:
                        sp.wait_ge(sampled.sem, sampled.at(b, PIECES))
                        hold(sp, held_sp1)
                        load_image(b + 1, (b + 1) % B, 1 - parity)
                    if s >= 2:
                        i = s - 2
                        sp.wait_ge(normed2.sem, normed2.at(b, i + 1))
                        sp.dma_start(t2_dram[bass.ds(b, 1), :, i, :].rearrange("a p c -> (a p) c"),
                                     t2[i % 3][:]).then_inc(t2_out[i % 3].sem, 16)
                sp.wait_ge(chosen.sem, chosen.at(b, 1))
                sp.dma_start(pm_dram[bass.ds(b, 1)].rearrange("a e n -> (a e) n"), logit[:])\
                  .then_inc(route_out.sem, 16)
                sp.dma_start(rz_dram[bass.ds(b, 1)].rearrange("a e n -> (a e) n"), rz[:])\
                  .then_inc(route_out.sem, 16)
                sp.wait_ge(pooled_ev.sem, pooled_ev.at(b, 1))
                sp.dma_start(pooled_dram[bass.ds(b, 1)].rearrange("a e n -> (a e) n"), pooled[:])\
                  .then_inc(route_out.sem, 16)
            sp.wait_ge(route_out.sem, route_out.at(B, 0))
            for r in range(3):
                sp.wait_ge(t2_out[r].sem, t2_out[r].at(B, 0))
            sp.wait_ge(table_in.sem, table_in.at(B + 1, 0))

        @block.gpsimd
        def _(pool):
            pool.memset(prob[0][:], 0.0).then_inc(zeroed, 1)
            for d in range(3):
                pool.memset(xs[d][:], 0.0).then_inc(zeroed, 1)
            pool.memset(nb_next[:], 0.0).then_inc(zeroed, 1)
            pool.memset(logit[:], 0.0).then_inc(zeroed, 1)
            for t in xt:
                pool.memset(t[:], 0.0).then_inc(zeroed, 1)
            pool.sem_inc(idx_copied.sem, idx_copied.primed)
            pool.wait_ge(border_in, 16 * 32)
            with pool.Fori(0, B // 2) as half:
              for parity in range(2):
                b = half * 2 + parity
                pool.wait_ge(indexed.sem, indexed.at(b, 1))
                pool.wait_ge(sampled.sem, sampled.at(b, 0))
                hold(pool, held_pool)
                pool.tensor_copy(idx[:], idx_next[:]).then_inc(idx_copied.sem, 1)
                pool.wait_ge(idx_copied.sem, idx_copied.at(b, 1))
                pool.wait_ge(table_in.sem, table_in.at(b, 4))
                for i in range(TILES):
                    pool.wait_ge(sampled.sem, sampled.at(b, PIECES * (i - RING + 1)))
                    hold(pool, held_pool)
                    for n in range(TAPS):
                        pool.indirect_dma_start(
                            g[i % RING][:, n, :], None, pair_table[parity],
                            bass.IndirectOffsetOnAxis(ap=idx[:, i * TAPS + n:i * TAPS + n + 1], axis=0),
                        ).then_inc(gathered[i % RING].sem, 16)

        @block.scalar
        def _(act):
            for sig in (shifted, shift_ev, rs_copied, scaled, smp_ev, xnt_ev, proj_ev, exp_done,
                        xft_ev, logit_ev, lexp_done, pm_ev, link_xs):
                act.sem_inc(sig.sem, sig.primed)

            act.wait_ge(setup_mm, 1)
            act.activation(offw_t[:], bank_s[0][:, 0:TAPS * 18].rearrange("p (t k) -> p t k", k=18),
                           ACT.Copy).then_inc(setup_ev, 1)
            for n in range(TAPS):
                act.wait_ge(setup_mm, 2 + n)
                act.activation(convw_t[:, n, :], bank_t[n % 2][:, 0:P], ACT.Copy).then_inc(setup_ev, 1)
            act.wait_ge(setup_mm, 2 + TAPS)
            act.activation(wv_t[:], bank_s[1][:, 0:P], ACT.Copy).then_inc(setup_ev, 1)
            act.activation(gate_t[:], bank_s[1][:, P:P + E], ACT.Copy).then_inc(setup_ev, 1)
            act.activation(wqk[:], bank_s[1][:, 2 * P:3 * P], ACT.Copy).then_inc(setup_ev, 1)

            def shift_images(k):
                act.wait_ge(affine_done.sem, affine_done.at(k, 1))
                raw = xs[1][:, W:W + N].rearrange("p (y x) -> p y x", x=W)
                left = xs[0][:, W:W + N].rearrange("p (y x) -> p y x", x=W)
                right = xs[2][:, W:W + N].rearrange("p (y x) -> p y x", x=W)
                nb = nb_next[:, TAPS - 1:TAPS]
                act.activation(left[:, :, 1:W], raw[:, :, 0:W - 1], ACT.Identity, bias=nb,
                               scale=rs_next[:, 0:1]).then_inc(link_xs.sem, 1)
                act.activation(right[:, :, 0:W - 1], raw[:, :, 1:W], ACT.Identity, bias=nb,
                               scale=rs_next[:, 0:1]).then_inc(link_xs.sem, 1)
                act.wait_ge(link_xs.sem, link_xs.at(k, 2))
                act.activation(xs[1][:, W:W + N], xs[1][:, W:W + N], ACT.Identity, bias=nb,
                               scale=rs_next[:, 0:1]).then_inc(shifted.sem, 1)

            def scale_first(b, i):
                act.wait_ge(gathered[i % RING].sem, gathered[i % RING].at(b, TAPS * (i // RING + 1)))
                act.wait_ge(smp_tp.sem, smp_tp.at(b, PIECES * (i - 1) if i >= 2 else 0))
                if i == 0:
                    act.wait_ge(rs_copied.sem, rs_copied.at(b, 1))
                for n in range(TAPS):
                    last = act.activation(smp[i % 2][:, n, :], g[i % RING][:, n, 0:C], ACT.Copy,
                                          scale=wa[:, i, n:n + 1])
                last.then_inc(scaled.sem, 1)

            shift_images(0)
            with act.Fori(0, B) as b:
                act.wait_ge(indexed.sem, indexed.at(b, 1))
                act.wait_ge(smp_ev.sem, smp_ev.at(b, 0))
                act.wait_ge(scaled.sem, scaled.at(b, 0))
                act.activation(rs[:], rs_next[:], ACT.Copy)
                act.activation(wa[:], wa_next[:], ACT.Copy).then_inc(rs_copied.sem, 1)
                act.wait_ge(shift_mm.sem, shift_mm.at(b, 1))
                act.activation(shift[:], small_ps[0:TAPS, :], ACT.Copy).then_inc(shift_ev.sem, 1)
                scale_first(b, 0)
                for s in range(TILES + 3):
                    if s < TILES:
                        for p in range(PIECES):
                            q = PIECES * s + p
                            act.wait_ge(smp_tp.sem, smp_tp.at(b, q + 1))
                            last = act.activation(smp_t[p][:], ring_use(True, q)[:, 0:3 * P], ACT.Copy,
                                                  scale=rs[:, 0:1])
                            if p == PIECES - 1:
                                last = act.activation(u_t[s % 2][:], ring_use(True, q)[0:TAPS, 3 * P:], ACT.Copy)
                            last.then_inc(smp_ev.sem, 1)
                    if s + 1 < TILES:
                        scale_first(b, s + 1)
                    if s == NORM_STEP + 1:
                        shift_images(b + 1)
                    if s >= 3:
                        i = s - 3
                        act.wait_ge(xft_tp.sem, xft_tp.at(b, i + 1))
                        act.activation(xf_t[:], xft_ps, ACT.Copy).then_inc(xft_ev.sem, 1)
                        act.wait_ge(logit_mm.sem, logit_mm.at(b, i + 1))
                        if i == 0:
                            act.wait_ge(pm_tp.sem, pm_tp.at(b, 0))
                            act.wait_ge(route_out.sem, route_out.at(b, 0))
                        act.activation(logit[:, i * P:(i + 1) * P] if i < TILES - 1
                                       else logit[:, i * P:i * P + LAST],
                                       logit_ps if i < TILES - 1 else logit_ps[:, 0:LAST],
                                       ACT.Identity, bias=gate_bias[:, 0:1]).then_inc(logit_ev.sem, 1)
                    if s < TILES:
                        act.wait_ge(xnt_tp.sem, xnt_tp.at(b, s + 1))
                        act.activation(keys[:, s * P:(s + 1) * P], xnt_ps, ACT.Copy).then_inc(xnt_ev.sem, 1)
                        act.wait_ge(proj_done.sem, proj_done.at(b, s + 1))
                        act.activation(vals[:, s, :], val_ps, ACT.Copy)
                        act.activation(qt[s % 2][:], qt_ps, ACT.Copy, scale=SCALE).then_inc(proj_ev.sem, 1)
                    if 1 <= s <= TILES:
                        i = s - 1
                        act.wait_ge(max_done.sem, max_done.at(b, i + 1))
                        act.activation(prob[i % 2][:, 0:(i + 1) * P], prob[i % 2][:, 0:(i + 1) * P],
                                       ACT.Exp, bias=nmax[i % 2][:, 1:2],
                                       accum_out=total[i % 2][:, 0:1]).then_inc(exp_done.sem, 1)
                act.wait_ge(lmax_done.sem, lmax_done.at(b, 1))
                act.activation(logit[:, 0:N], logit[:, 0:N], ACT.Exp, bias=lmax[:, 1:2],
                               accum_out=zsum[:, 0:1]).then_inc(lexp_done.sem, 1)
                for q in range(PMG):
                    n = min(8, TILES - 8 * q)
                    act.wait_ge(pm_tp.sem, pm_tp.at(b, q + 1))
                    act.activation(pm_tok[:, 8 * q:8 * q + n, :],
                                   bank_s[q % 2][:, 0:n * E].rearrange("p (t e) -> p t e", e=E),
                                   ACT.Copy).then_inc(pm_ev.sem, 1)

        @block.vector
        def _(dve):
            for sig in (stats_done, affine_done, indexed, u_copied, sampled, normed, score_ev, max_done,
                        prob_ev, normed2, lmax_done, chosen, rz_done, pooled_ev, link_prep,
                        link_norm, link_max, link_norm2, link_route):
                dve.sem_inc(sig.sem, sig.primed)
            prep, norm = Link(dve, link_prep), Link(dve, link_norm)
            lmx, norm2, route = Link(dve, link_max), Link(dve, link_norm2), Link(dve, link_route)
            dve.wait_ge(weights_in, 16 * 14)
            for n in range(3):
                dve.memset(newton[:, n:n + 1], float(4 ** (3 - n)))
            dve.drain()

            def rsqrt(link, w, var):
                v, y, a = w[:, 8:11], w[:, 11:12], w[:, 12:13]
                link(dve.scalar_tensor_tensor(v, var.broadcast_to([P, 3]), EPS, newton[:], ALU.add, ALU.mult))
                link(dve.tensor_scalar(y.bitcast(I32), v[:, 2:3].bitcast(I32), -0.5, RSQRT_GUESS, ALU.mult, ALU.add))
                for n in range(3):
                    link(dve.scalar_tensor_tensor(a, y, v[:, n:n + 1], y, ALU.mult, ALU.mult))
                    link(dve.scalar_tensor_tensor(y, a, 3.0, y, ALU.subtract, ALU.mult, reverse0=(n == 0)))
                return y

            def layer_norm(link, src, dst, w):
                link(dve.bn_stats(w[:, 0:6], src))
                hold(dve, held_dve)
                link(dve.bn_aggr(w[:, 6:8], w[:, 0:6]))
                y = rsqrt(link, w, w[:, 7:8])
                return dve.tensor_scalar(dst, src, w[:, 6:7], y, ALU.subtract, ALU.mult)

            def image_stats(k):
                prep.start(k)
                dve.wait_ge(x_in.sem, x_in.at(k, 1))
                for c in range(STATS):
                    w = N // STATS
                    last = dve.bn_stats(bn[:, c, :], xs[1][:, W + c * w:W + (c + 1) * w])
                prep(last)
                dve.wait_ge(gstat_done.sem, gstat_done.at(k, 0))
                hold(dve, held_dve)
                prep(dve.bn_aggr(mv[:], bn[:].rearrange("p a k -> p (a k)")))
                dve.scalar_tensor_tensor(mv[:, 1:2], mv[:, 0:1], mv[:, 0:1], mv[:, 1:2], ALU.mult, ALU.add)\
                   .then_inc(stats_done.sem, 1)

            def affine(k):
                dve.wait_ge(gstat_done.sem, gstat_done.at(k, 1))
                prep(dve.tensor_copy(gstat[:], small_ps[:, 0:2]))
                prep(dve.scalar_tensor_tensor(gvar[:, 0:1], gstat[:, 0:1], gstat[:, 0:1], gstat[:, 1:2],
                                              ALU.mult, ALU.subtract))
                prep(dve.tensor_scalar(gvar[:, 1:2], gvar[:, 0:1], -1.0, None, ALU.mult))
                y = rsqrt(prep, gvar, gvar[:, 1:2])
                dve.wait_ge(shift_mm.sem, shift_mm.at(k, 0))
                dve.wait_ge(rs_copied.sem, rs_copied.at(k, 0))
                prep(dve.tensor_copy(rs_next[:], y))
                dve.scalar_tensor_tensor(nb_next[:, TAPS - 1:TAPS], gstat[:, 0:1], -1.0, rs_next[:],
                                         ALU.mult, ALU.mult).then_inc(affine_done.sem, 1)

            def index(k):
                dve.wait_ge(offsets_done.sem, offsets_done.at(k, 1))
                dve.wait_ge(affine_done.sem, affine_done.at(k, 1))
                both = lambda t: t.rearrange("p t k -> p (t k)")
                bias = off_bias[:].unsqueeze(1).broadcast_to([P, TILES, 18])
                prep(dve.tensor_tensor(pos, off_ps, bias, ALU.add))
                prep(dve.tensor_tensor(pos, pos, base[:], ALU.add))
                prep(dve.tensor_scalar(pos, pos, 0.0, float(HP - 1), ALU.max, ALU.min))
                prep(dve.tensor_copy(qi, pos))
                prep(dve.tensor_copy(qf, qi))
                prep(dve.tensor_tensor(tmp, qf, pos, ALU.is_gt))
                prep(dve.tensor_tensor(qf, qf, tmp, ALU.subtract))
                prep(dve.tensor_tensor(pos, pos, qf, ALU.subtract))
                qy, qx = qf[:, :, 0:TAPS], qf[:, :, TAPS:]
                fy, fx = pos[:, :, 0:TAPS], pos[:, :, TAPS:]
                prep(dve.tensor_scalar(eq, fx, 0.0, None, ALU.is_equal))
                prep(dve.tensor_tensor(fx1, fx, eq, ALU.add))
                prep(dve.tensor_scalar(om, fy, -1.0, 1.0, ALU.mult, ALU.add))
                dve.wait_ge(rs_copied.sem, rs_copied.at(k, 0))
                dve.wait_ge(u_copied.sem, u_copied.at(k, 0))
                dve.wait_ge(idx_copied.sem, idx_copied.at(k, 0))
                prep(dve.tensor_tensor(wa_next[:], om, fx1, ALU.mult))
                prep(dve.tensor_scalar(om, fx, -1.0, 1.0, ALU.mult, ALU.add))
                prep(dve.tensor_tensor(wb_next[:], om, fy, ALU.mult))
                a = tmp[:, :, 0:TAPS]
                prep(dve.scalar_tensor_tensor(a, qy, float(WP), qx, ALU.mult, ALU.add))
                prep(dve.scalar_tensor_tensor(idx_next[:].rearrange("p (t k) -> p t k", k=TAPS), eq,
                                              float(HP * WP), a, ALU.mult, ALU.add))
                within = lambda out, what, op, bound, w: prep(
                    dve.scalar_tensor_tensor(out, what, bound, w, op, ALU.mult))
                within(u_next[:], qy, ALU.is_ge, 1.0, wa_next[:])
                within(u_next[:], qy, ALU.is_le, float(H), u_next[:])
                prep(dve.tensor_tensor(a, qx, eq, ALU.subtract))
                within(u_next[:], a, ALU.is_ge, 0.0, u_next[:])
                within(u_next[:], a, ALU.is_le, float(W - 1), u_next[:])
                d = tmp[:, :, TAPS:]
                within(d, qy, ALU.is_le, float(H - 1), wb_next[:])
                within(d, qx, ALU.is_ge, 1.0, d)
                within(d, qx, ALU.is_le, float(W), d)
                dve.tensor_tensor(u_next[:], u_next[:], d, ALU.add).then_inc(indexed.sem, 1)
                assert prep.n == link_prep.per, prep.n

            def add_second(b, i):
                dve.wait_ge(scaled.sem, scaled.at(b, i + 1))
                for p in range(PIECES):
                    for n in range(3 * p, 3 * p + 3):
                        last = dve.scalar_tensor_tensor(
                            smp[i % 2][:, n, :], g[i % RING][:, n, C:], wb[:, i, n:n + 1],
                            smp[i % 2][:, n, :], ALU.mult, ALU.add)
                    last.then_inc(sampled.sem, 1)

            image_stats(0)
            affine(0)
            index(0)
            with dve.Fori(0, B) as b:
                dve.wait_ge(indexed.sem, indexed.at(b, 1))
                dve.wait_ge(smp_tp.sem, smp_tp.at(b, 0))
                dve.wait_ge(sampled.sem, sampled.at(b, 0))
                dve.tensor_copy(wb[:], wb_next[:])
                dve.tensor_copy(u[:], u_next[:]).then_inc(u_copied.sem, 1)
                dve.wait_ge(u_copied.sem, u_copied.at(b, 1))
                add_second(b, 0)
                norm.start(b)
                lmx.start(b)
                norm2.start(b)
                route.start(b)
                for s in range(TILES + 2):
                    if s < TILES:
                        dve.wait_ge(conv_done.sem, conv_done.at(b, s + 1))
                        dve.wait_ge(xt_in[s % RING].sem, xt_in[s % RING].at(b, s // RING + 1))
                        norm(dve.tensor_tensor(t1[s % 3][:], conv_ps, xt[s % RING][:], ALU.add))
                        dve.wait_ge(xnt_tp.sem, xnt_tp.at(b, max(s - 1, 0)))
                        layer_norm(norm, t1[s % 3][:], xn[s % 2][:], ln[s % 2]).then_inc(normed.sem, 1)
                    if s == STATS_STEP:
                        image_stats(b + 1)
                    if s == NORM_STEP:
                        affine(b + 1)
                    if s == INDEX_STEP:
                        index(b + 1)
                    if 1 <= s <= TILES:
                        i = s - 1
                        r = i % 2
                        if i >= 2:
                            dve.wait_ge(prob_tp.sem, prob_tp.at(b, chunks_before(i - 1)))
                        else:
                            dve.wait_ge(pooled_ev.sem, pooled_ev.at(b, 0))
                            dve.wait_ge(prob_tp.sem, prob_tp.at(b, 0))
                        cs = chunks_of(i)
                        for j, (k0, w) in enumerate(cs):
                            q = chunks_before(i) + j
                            dve.wait_ge(scored.sem, scored.at(b, q + 1))
                            hold(dve, held_dve)
                            m = mask[:, CHUNK + P - w:] if j == len(cs) - 1 else mask[:, 0:w]
                            dve.tensor_tensor_reduce(prob[r][:, k0:k0 + w], bank_s[q % 2][:, 0:w], m, 1.0, NEG,
                                                     ALU.add, ALU.max, cmax[r][:, j:j + 1])\
                               .then_inc(score_ev.sem, 1)
                        dve.wait_ge(score_ev.sem, score_ev.at(b, chunks_before(i + 1)))
                        lmx(dve.tensor_reduce(nmax[r][:, 0:1], cmax[r][:, 0:len(cs)], AXX, ALU.max))
                        dve.tensor_scalar(nmax[r][:, 1:2], nmax[r][:, 0:1], -1.0, None, ALU.mult)\
                           .then_inc(max_done.sem, 1)
                    if s + 1 < TILES:
                        add_second(b, s + 1)
                    if s >= 2:
                        i = s - 2
                        r = i % 2
                        for j, (k0, w) in enumerate(chunks_of(i)):
                            q = chunks_before(i) + j
                            dve.wait_ge(prob_tp.sem, prob_tp.at(b, q + 1))
                            dve.tensor_copy(prob_t[q % 2][:, 0:w], ring_use(False, q)[:, 0:w])\
                               .then_inc(prob_ev.sem, 1)
                        dve.wait_ge(attended.sem, attended.at(b, i + 1))
                        dve.wait_ge(exp_done.sem, exp_done.at(b, i + 1))
                        dve.wait_ge(t2_out[i % 3].sem, t2_out[i % 3].at(b, i // 3))
                        norm2(dve.reciprocal(total[r][:], total[r][:]))
                        norm2(dve.scalar_tensor_tensor(t2[i % 3][:], bank_o[:, 0:P], total[r][:, 0:1],
                                                       t1[i % 3][:], ALU.mult, ALU.add))
                        if i == 0:
                            dve.wait_ge(pooled_mm.sem, pooled_mm.at(b, 0))
                        layer_norm(norm2, t2[i % 3][:], xf[:, i, :], ln[i % 2])\
                            .then_inc(normed2.sem, 1)
                assert norm.n == link_norm.per and norm2.n == link_norm2.per and lmx.n == link_max.per
                dve.wait_ge(logit_ev.sem, logit_ev.at(b, TILES))
                route(dve.tensor_reduce(lmax[:, 0:1], logit[:, 0:N], AXX, ALU.max))
                dve.tensor_scalar(lmax[:, 1:2], lmax[:, 0:1], -1.0, None, ALU.mult).then_inc(lmax_done.sem, 1)
                dve.wait_ge(route_out.sem, route_out.at(b, 0))
                dve.wait_ge(lexp_done.sem, lexp_done.at(b, 1))
                dve.reciprocal(rz[:], zsum[:]).then_inc(rz_done.sem, 1)
                route(dve.max(top[:], logit[:, 0:N]))
                hold(dve, held_dve)
                route(dve.match_replace(rest, top[:], logit[:, 0:N], 0.0))
                dve.wait_ge(rz_done.sem, rz_done.at(b, 1))
                dve.tensor_tensor(logit[:, 0:N], logit[:, 0:N], rest, ALU.subtract).then_inc(chosen.sem, 1)
                dve.wait_ge(pooled_mm.sem, pooled_mm.at(b, 1))
                dve.tensor_scalar(pooled[:], bank_o[0:E, 0:P], rz[:, 0:1], None, ALU.mult)\
                   .then_inc(pooled_ev.sem, 1)

        @block.tensor
        def _(pe):
            for sig in (gstat_done, offsets_done, shift_mm, smp_tp, conv_done, xnt_tp, proj_done,
                        scored, prob_tp, attended, xft_tp, logit_mm, pm_tp, pooled_mm):
                pe.sem_inc(sig.sem, sig.primed)
            pe.wait_ge(weights_in, 16 * 14)
            for n in range(TAPS):
                last = pe.transpose(bank_s[0][:, n * 18:(n + 1) * 18], raw_off.rearrange("o (c t) -> o c t", t=TAPS)[:, :, n], ident[0:18, 0:18])
            last.then_inc(setup_mm, 1)
            for n in range(TAPS):
                if n >= 2:
                    pe.wait_ge(setup_ev, n)
                pe.transpose(bank_t[n % 2][:, 0:P], raw_conv.rearrange("o (c t) -> o c t", t=TAPS)[:, :, n], ident[:]).then_inc(setup_mm, 1)
            pe.transpose(bank_s[1][:, 0:P], vals[:, 2, :], ident[:])
            pe.transpose(bank_s[1][:, P:P + E], vals[0:E, 3, :], ident[0:E, 0:E])
            pe.matmul(bank_s[1][:, 2 * P:3 * P], vals[:, 0, :], vals[:, 1, :],
                      start=True, stop=True).then_inc(setup_mm, 1)

            def group_stats(k):
                pe.wait_ge(stats_done.sem, stats_done.at(k, 1))
                pe.wait_ge(shift_ev.sem, shift_ev.at(k, 0))
                pe.matmul(small_ps[:, 0:2], group[:], mv[:], start=True, stop=True)\
                  .then_inc(gstat_done.sem, 1)

            def offsets(k, tiles):
                for i in tiles:
                    if i == 0:
                        pe.wait_ge(indexed.sem, indexed.at(k, 0))
                        pe.wait_ge(shifted.sem, shifted.at(k, 1))
                    for n in range(TAPS):
                        dy, dx = n // 3 - 1, n % 3
                        at = W + i * P + dy * W
                        last = pe.matmul(off_ps[:, i, :], xs[dx][:, at:at + P], offw_t[:, n, :],
                                         start=(n == 0), stop=(n == TAPS - 1))
                    if i == TILES - 1:
                        last.then_inc(offsets_done.sem, 1)

            pe.wait_ge(zeroed, ZEROED)
            group_stats(0)
            pe.wait_ge(setup_ev, 4 + TAPS)
            offsets(0, range(TILES))
            with pe.Fori(0, B) as b:
                pe.wait_ge(indexed.sem, indexed.at(b, 1))
                pe.wait_ge(normed.sem, normed.at(b, 0))
                for n in range(TAPS):
                    last = pe.matmul(small_ps[0:TAPS, :], nb_next[:, TAPS - 1 - n:2 * TAPS - 1 - n],
                                     convw_t[:, n, :], start=(n == 0), stop=(n == TAPS - 1))
                last.then_inc(shift_mm.sem, 1)
                for s in range(TILES + 3):
                    if s < TILES:
                        if s == 0:
                            pe.wait_ge(u_copied.sem, u_copied.at(b, 1))
                            pe.wait_ge(shift_ev.sem, shift_ev.at(b, 1))

                        def products(p):
                            pe.wait_ge(smp_ev.sem, smp_ev.at(b, PIECES * s + p + 1))
                            for n in range(3):
                                pe.matmul(conv_ps, smp_t[p][:, n * P:(n + 1) * P],
                                          convw_t[:, 3 * p + n, :], start=(p == 0 and n == 0), stop=False)

                        for p in range(PIECES):
                            q = PIECES * s + p
                            pe.wait_ge(sampled.sem, sampled.at(b, q + 1))
                            wait_ring(pe, b, True, q)
                            bank = ring_use(True, q)
                            for n in range(3):
                                last = pe.transpose(bank[:, n * P:(n + 1) * P], smp[s % 2][:, 3 * p + n, :],
                                                    ident[:])
                            if p == PIECES - 1:
                                last = pe.transpose(bank[0:TAPS, 3 * P:], u[:, s, :], ident[:])
                            last.then_inc(smp_tp.sem, 1)
                            if p == 1:
                                pe.wait_ge(normed.sem, normed.at(b, s))
                                if s == NORM_STEP + 1:
                                    pe.wait_ge(affine_done.sem, affine_done.at(b + 1, 1))
                            if p >= 1:
                                products(p - 1)
                        products(PIECES - 1)
                        pe.matmul(conv_ps, u_t[s % 2][:], shift[:], start=False, stop=True)\
                          .then_inc(conv_done.sem, 1)
                    if s >= 3:
                        i = s - 3
                        pe.wait_ge(normed2.sem, normed2.at(b, i + 1))
                        pe.wait_ge(proj_ev.sem, proj_ev.at(b, min(s, TILES)))
                        pe.wait_ge(logit_ev.sem, logit_ev.at(b, i))
                        pe.transpose(xft_ps, xf[:, i, :], ident[:]).then_inc(xft_tp.sem, 1)
                        pe.wait_ge(xft_ev.sem, xft_ev.at(b, i + 1))
                        pe.matmul(logit_ps, gate_t[:], xf_t[:], start=True, stop=True).then_inc(logit_mm.sem, 1)
                    if s == NORM_STEP:
                        pe.wait_ge(normed.sem, normed.at(b, s + 1))
                        group_stats(b + 1)
                    if s >= OFFSET_STEP0:
                        t0 = (s - OFFSET_STEP0) * OFFSETS_PER_STEP
                        offsets(b + 1, range(t0, min(t0 + OFFSETS_PER_STEP, TILES)))
                    if 1 <= s <= TILES:
                        i = s - 1
                        pe.wait_ge(proj_ev.sem, proj_ev.at(b, i + 1))
                        for j, (k0, w) in enumerate(chunks_of(i)):
                            q = chunks_before(i) + j
                            if q == 0:
                                pe.wait_ge(pm_ev.sem, pm_ev.at(b, 0))
                            pe.wait_ge(score_ev.sem, score_ev.at(b, max(q - 1, 0)))
                            pe.matmul(bank_s[q % 2][:, 0:w], qt[i % 2][:], keys[:, k0:k0 + w],
                                      start=True, stop=True).then_inc(scored.sem, 1)
                    if s < TILES:
                        pe.wait_ge(normed.sem, normed.at(b, s + 1))
                        pe.wait_ge(proj_ev.sem, proj_ev.at(b, s))
                        pe.wait_ge(logit_ev.sem, logit_ev.at(b, max(s - 2, 0)))
                        pe.transpose(xnt_ps, xn[s % 2][:], ident[:]).then_inc(xnt_tp.sem, 1)
                        pe.wait_ge(xnt_ev.sem, xnt_ev.at(b, s + 1))
                        kt = keys[:, s * P:(s + 1) * P]
                        pe.matmul(val_ps, kt, wv_t[:], start=True, stop=True)
                        pe.matmul(qt_ps, wqk[:], kt, start=True, stop=True).then_inc(proj_done.sem, 1)
                    if 2 <= s <= TILES + 1:
                        i = s - 2
                        cs = chunks_of(i)
                        pe.wait_ge(exp_done.sem, exp_done.at(b, i + 1))

                        def attend(j):
                            k0, w = cs[j]
                            q = chunks_before(i) + j
                            pe.wait_ge(prob_ev.sem, prob_ev.at(b, q + 1))
                            for n in range(w // P):
                                t = k0 // P + n
                                last = pe.matmul(bank_o[:, 0:P], prob_t[q % 2][:, n * P:(n + 1) * P],
                                                 vals[:, t, :], start=(t == 0), stop=(t == i))
                            if t == i:
                                last.then_inc(attended.sem, 1)

                        for j, (k0, w) in enumerate(cs):
                            q = chunks_before(i) + j
                            wait_ring(pe, b, False, q)
                            for n in range(w // P):
                                last = pe.transpose(ring_use(False, q)[:, n * P:(n + 1) * P],
                                                    prob[i % 2][:, k0 + n * P:k0 + (n + 1) * P], ident[:])
                            last.then_inc(prob_tp.sem, 1)
                            if j == 1:
                                pe.wait_ge(normed2.sem, normed2.at(b, i))
                            if j >= 1:
                                attend(j - 1)
                        if len(cs) == 1:
                            pe.wait_ge(normed2.sem, normed2.at(b, i))
                            if i == 0:
                                pe.wait_ge(pooled_ev.sem, pooled_ev.at(b, 0))
                        attend(len(cs) - 1)
                pe.wait_ge(chosen.sem, chosen.at(b, 1))
                for q in range(PMG):
                    pe.wait_ge(pm_ev.sem, pm_ev.at(b, max(q - 1, 0)))
                    hold(pe, held_pe)
                    for n in range(min(8, TILES - 8 * q)):
                        t = 8 * q + n
                        last = pe.transpose(bank_s[q % 2][:, n * E:(n + 1) * E],
                                            logit[:, t * P:(t + 1) * P], ident[0:E, 0:E])
                    last.then_inc(pm_tp.sem, 1)
                for t in range(TILES):
                    if t % 8 == 0:
                        pe.wait_ge(pm_ev.sem, pm_ev.at(b, t // 8 + 1))
                    last = pe.matmul(bank_o[0:E, 0:P], pm_tok[:, t, :], xf[:, t, :],
                                     start=(t == 0), stop=(t == TILES - 1))
                last.then_inc(pooled_mm.sem, 1)



def second_part(nc, w1, w2, b1_t, b2, ident, t2_dram, pm_dram, pooled_dram, rz_dram, out):
    G = 4
    SLOTS = 4
    J = HID // P
    ROUNDS = E // (G * SLOTS)
    CH = [(k, min(CHUNK, N - k)) for k in range(0, N, CHUNK)]
    with ExitStack() as ctx:
        def sb(name, shape):
            return ctx.enter_context(nc.sbuf_tensor(name, shape, F32))

        def psum(name):
            return ctx.enter_context(nc.psum_tensor(name, [P, 512], F32))

        def sem(name):
            return ctx.enter_context(nc.semaphore(name))

        def signal(name, per_round, unit=1, before=0):
            return Signal(sem(name), per_round, unit, before)

        w1s = [sb(f"w1s{r}", [P, G, HID]) for r in range(SLOTS)]
        w2s = [sb(f"w2s{r}", [P, G, J, C]) for r in range(SLOTS)]
        pl = sb("pl", [P, 4, C])
        pooled_t = sb("pooled_t", [P, B, E])
        rz = sb("rz_all", [E, B])
        pre = [sb(f"pre{r}", [P, G, J, B]) for r in range(2)]
        act_h = [sb(f"act_h{r}", [P, G, J, B]) for r in range(2)]
        out_t = sb("out_t", [P, B, E])
        biased = sb("biased", [E, B, C])
        out_w = sb("out_w", [E, B, C])
        out_cur = [sb(f"out_cur{r}", [E, C]) for r in range(2)]
        pm = [sb(f"pm{r}", [E, NP]) for r in range(2)]
        t2 = [sb(f"t2s{r}", [P, TILES, C]) for r in range(2)]
        res = [sb(f"res{r}", [P, N]) for r in range(2)]
        bank_h = [psum(f"bank_h{r}") for r in range(2)]
        bank_y = [psum(f"bank_y{r}") for r in range(2)]
        bank_r = [psum(f"bank_r{r}") for r in range(4)]

        held_sp = sem("held_sp")
        small_in, pooled_tp, pooled_ev = sem("small_in"), sem("pooled_tp"), sem("pooled_ev2")
        w_in = [signal(f"w_in{r}", 2, 16) for r in range(SLOTS)]
        hidden = signal("hidden", SLOTS)
        hidden_b = signal("hidden_b", SLOTS)
        gelued = signal("gelued", SLOTS)
        outed = signal("outed", SLOTS, before=SLOTS)
        out_ev = signal("out_ev", SLOTS)
        out_tp, out_b, out_ready = sem("out_tp"), sem("out_b"), sem("out_ready")
        image_in = [signal(f"image_in{r}", 2, 16) for r in range(2)]
        cur_done = signal("cur_done", 2)
        summed = signal("summed", 2 * len(CH))
        res_a = signal("res_a", 2 * len(CH) // 2)
        res_d = signal("res_d", 2 * len(CH) // 2)
        stored = [signal(f"stored{r}", 1, 16) for r in range(2)]
        mine = lambda q: (res_d if q % 2 == 0 else res_a, q // 2)

        block = ctx.enter_context(nc.Block())

        @block.sync
        def _(sp):
            sp.dma_start(pl[:], pooled_dram.rearrange("b e c -> (b e) c").rearrange("(a p) c -> p a c", p=P))\
              .then_inc(small_in, 16)
            sp.dma_start(rz[:], rz_dram.rearrange("b e a -> e (b a)"), allow_slow_non_contiguous=True).then_inc(small_in, 16)
            for sig in (*w_in, *image_in, *stored):
                sp.sem_inc(sig.sem, sig.primed)
            with sp.Fori(0, ROUNDS) as k:
                for r in range(SLOTS):
                    sp.wait_ge(outed.sem, outed.at(k, r + 1 - SLOTS))
                    e0 = k * (SLOTS * G) + r * G
                    sp.dma_start(w1s[r][:], w1[bass.ds(e0, G), 0:C, :].rearrange("e c h -> c e h"))\
                      .then_inc(w_in[r].sem, 16)
                    sp.dma_start(w2s[r][:].rearrange("p e j o -> p e (j o)"),
                                 w2[bass.ds(e0, G), 0:HID, :].rearrange("e (p j) o -> p e (j o)", j=J))\
                      .then_inc(w_in[r].sem, 16)
            with sp.Fori(0, B // 2) as k:
                for r in range(2):
                    sp.wait_ge(summed.sem, summed.at(k, 0) if r == 0 else summed.at(k, 0))
                    at = k * 2 + r
                    sp.dma_start(pm[r][:], pm_dram[bass.ds(at, 1)].rearrange("a e n -> (a e) n"))\
                      .then_inc(image_in[r].sem, 16)
                    sp.dma_start(t2[r][:], t2_dram[bass.ds(at, 1)].rearrange("a p t c -> (a p) t c"))\
                      .then_inc(image_in[r].sem, 16)
                for r in range(2):
                    at = k * 2 + r
                    n = len(CH) * (r + 1)
                    sp.wait_ge(res_d.sem, res_d.at(k, (n + 1) // 2))
                    hold(sp, held_sp)
                    sp.wait_ge(res_a.sem, res_a.at(k, n // 2))
                    sp.dma_start(out[bass.ds(at, 1)].rearrange("a c n -> (a c) n"), res[r][:])\
                      .then_inc(stored[r].sem, 16)
            for r in range(2):
                sp.wait_ge(stored[r].sem, stored[r].at(B // 2, 0))

        @block.scalar
        def _(act):
            for sig in (gelued, res_a):
                act.sem_inc(sig.sem, sig.primed)
            act.wait_ge(pooled_tp, 1)
            act.activation(pooled_t[:].rearrange("p b e -> p (b e)"), bank_r[0][:], ACT.Copy)\
               .then_inc(pooled_ev, 1)
            with act.Fori(0, ROUNDS) as k:
                for r in range(SLOTS):
                    act.wait_ge(hidden_b.sem, hidden_b.at(k, r + 1))
                    act.wait_ge(outed.sem, outed.at(k, r - 1))
                    act.activation(act_h[r % 2][:], pre[r % 2][:], ACT.Gelu).then_inc(gelued.sem, 1)
            with act.Fori(0, B // 2) as k:
                for r in range(2):
                    for j, (k0, w) in enumerate(CH):
                        q = r * len(CH) + j
                        if q % 2 == 1:
                            act.wait_ge(summed.sem, summed.at(k, q + 1))
                            act.wait_ge(stored[r].sem, stored[r].at(k, 0))
                            act.activation(res[r][:, k0:k0 + w], bank_r[q % 4][:, 0:w], ACT.Copy)\
                               .then_inc(res_a.sem, 1)

        @block.vector
        def _(dve):
            for sig in (hidden_b, out_ev, cur_done, res_d):
                dve.sem_inc(sig.sem, sig.primed)
            with dve.Fori(0, ROUNDS) as k:
                for r in range(SLOTS):
                    e0 = k * (SLOTS * G) + r * G
                    dve.wait_ge(hidden.sem, hidden.at(k, r + 1))
                    dve.wait_ge(gelued.sem, gelued.at(k, max(r - 1, 0)))
                    bias = b1_t[:, bass.ds(e0, G), :].unsqueeze(3).broadcast_to([P, G, J, B])
                    dve.tensor_tensor(pre[r % 2][:], bank_h[r % 2][:, 0:G * J * B]
                                      .rearrange("p (e j b) -> p e j b", e=G, j=J), bias, ALU.add)\
                       .then_inc(hidden_b.sem, 1)
                    dve.wait_ge(outed.sem, outed.at(k, r + 1))
                    dve.tensor_scalar(out_t[:, :, bass.ds(e0, G)],
                                      bank_y[r % 2][:, 0:G * B].rearrange("p (e b) -> p b e", e=G), 1.0, None,
                                      ALU.mult).then_inc(out_ev.sem, 1)
            dve.wait_ge(small_in, 32)
            for b in range(B):
                dve.wait_ge(out_tp, b // 4 + 1)
                dve.tensor_tensor(biased[:, b, :], bank_r[b // 4][0:E, (b % 4) * C:(b % 4 + 1) * C], b2[:],
                                  ALU.add).then_inc(out_b, 1)
            for b in range(B):
                dve.wait_ge(out_b, b + 1)
                dve.tensor_scalar(out_w[:, b, :], biased[:, b, :], rz[:, b:b + 1], None, ALU.mult)\
                   .then_inc(out_ready, 1)
            dve.wait_ge(out_ready, B)
            with dve.Fori(0, B // 2) as k:
                for r in range(2):
                    dve.wait_ge(summed.sem, summed.at(k, 0))
                    dve.wait_ge(out_ready, B)
                    dve.tensor_copy(out_cur[r][:].rearrange("e (a c) -> e a c", a=1),
                                    out_w[:, bass.ds(k * 2 + r, 1), :]).then_inc(cur_done.sem, 1)
                for r in range(2):
                    for j, (k0, w) in enumerate(CH):
                        q = r * len(CH) + j
                        if q % 2 == 0:
                            dve.wait_ge(summed.sem, summed.at(k, q + 1))
                            dve.wait_ge(stored[r].sem, stored[r].at(k, 0))
                            dve.tensor_copy(res[r][:, k0:k0 + w], bank_r[q % 4][:, 0:w]).then_inc(res_d.sem, 1)

        @block.tensor
        def _(pe):
            for sig in (hidden, outed, summed):
                pe.sem_inc(sig.sem, sig.primed)
            pe.wait_ge(small_in, 32)
            for a in range(4):
                last = pe.transpose(bank_r[0][:, a * P:(a + 1) * P], pl[:, a, :], ident[:])
            last.then_inc(pooled_tp, 1)
            pe.wait_ge(pooled_ev, 1)
            with pe.Fori(0, ROUNDS) as k:
                def first(r):
                    e0 = k * (SLOTS * G) + r * G
                    pe.wait_ge(w_in[r].sem, w_in[r].at(k, 2))
                    pe.wait_ge(hidden_b.sem, hidden_b.at(k, max(r - 1, 0)))
                    for e in range(G):
                        x = pooled_t[:, :, bass.ds(e0 + e, 1)].rearrange("p b a -> p (b a)")
                        for j in range(J):
                            o = (e * J + j) * B
                            last = pe.matmul(bank_h[r % 2][:, o:o + B],
                                             w1s[r][:, e, :].rearrange("p (q j) -> p j q", j=J)[:, j, :], x,
                                             start=True, stop=True)
                    last.then_inc(hidden.sem, 1)

                def second(r):
                    pe.wait_ge(gelued.sem, gelued.at(k, r + 1))
                    pe.wait_ge(out_ev.sem, out_ev.at(k, max(r - 1, 0)))
                    for e in range(G):
                        for j in range(J):
                            last = pe.matmul(bank_y[r % 2][:, e * B:(e + 1) * B], w2s[r][:, e, j, :],
                                             act_h[r % 2][:, e, j, :], start=(j == 0), stop=(j == J - 1))
                    last.then_inc(outed.sem, 1)

                for r in range(SLOTS):
                    first(r)
                    if r >= 1:
                        second(r - 1)
                second(SLOTS - 1)
            pe.wait_ge(out_ev.sem, out_ev.at(ROUNDS, 0))
            for b in range(B):
                last = pe.transpose(bank_r[b // 4][0:E, (b % 4) * C:(b % 4 + 1) * C], out_t[:, b, :], ident[:])
                if b % 4 == 3:
                    last.then_inc(out_tp, 1)
            pe.wait_ge(out_b, B)
            with pe.Fori(0, B // 2) as k:
                for r in range(2):
                    pe.wait_ge(image_in[r].sem, image_in[r].at(k, 2))
                    pe.wait_ge(cur_done.sem, cur_done.at(k, 2))
                    for j, (k0, w) in enumerate(CH):
                        q = r * len(CH) + j
                        if q >= 4:
                            sig, n = mine(q - 4)
                            pe.wait_ge(sig.sem, sig.at(k, n + 1))
                        else:
                            pe.wait_ge(res_a.sem, res_a.at(k, 0))
                            pe.wait_ge(res_d.sem, res_d.at(k, 0))
                        bank = bank_r[q % 4]
                        pe.matmul(bank[:, 0:w], out_cur[r][:], pm[r][:, k0:k0 + w], start=True, stop=False)
                        for n in range(-(-w // P)):
                            m = min(P, w - n * P)
                            last = pe.matmul(bank[:, n * P:n * P + m], t2[r][:, k0 // P + n, :], ident[:, 0:m],
                                             start=False, stop=(n == -(-w // P) - 1))
                        last.then_inc(summed.sem, 1)


_WEIGHTS = ["L0_conv_offset_w", "L0_conv_offset_b", "L0_conv_conv_w", "L1_attn_Wq", "L1_attn_Wk", "L1_attn_Wv",
            "L1_ffn_gate_w", "L1_ffn_gate_b", "L1_ffn_weight1", "L1_ffn_weight2"]


def shape_constants():
    pixel = np.arange(TILES * P).reshape(TILES, P).T
    inside = pixel < N
    y = np.where(inside, pixel // W + 1, 1)
    x = np.where(inside, pixel % W + 1, 1)
    tap = np.arange(TAPS)
    base = np.concatenate([y[:, :, None] + (tap // 3 - 1), x[:, :, None] + (tap % 3 - 1)], axis=2)
    mask = np.zeros((P, CHUNK + P), np.float32)
    mask[:, CHUNK:] = np.where(np.arange(P)[None, :] > np.arange(P)[:, None], NEG, 0.0)
    of = np.arange(P) // (C // GROUPS)
    return [base.reshape(P, TILES * 18).astype(np.float32), np.eye(P, dtype=np.float32), mask,
            ((of[:, None] == of[None, :]) * (GROUPS / C)).astype(np.float32)]


def kernel(**inputs):
    import concourse.bacc as bacc
    from concourse.bass_utils import run_bass_kernel_spmd

    nc = bacc.Bacc("TRN2", target_bir_lowering=False, num_devices=1)
    x = np.ascontiguousarray(inputs["x"])
    given = [x.reshape(B, C, N), np.ascontiguousarray(x.transpose(0, 2, 3, 1)).reshape(B * N, C)]
    given += [np.ascontiguousarray(inputs[n]) for n in _WEIGHTS] + shape_constants()
    arrays, args = {}, []
    for i, a in enumerate(given):
        arrays[f"in_{i}_dram"] = a
        args.append(nc.dram_tensor(f"in_{i}_dram", a.shape, mybir.dt.from_np(a.dtype), kind="ExternalInput").ap())
    args.append(nc.dram_tensor("out_dram", (B, C, N), F32, kind="ExternalOutput").ap())
    hybrid_kernel(nc, *args)
    r = run_bass_kernel_spmd(nc, [arrays], core_ids=[0])
    return r.results[0]["out_dram"].reshape(B, C, H, W)
```
